# Optimizing a Trainium2 kernel written in Bass

```python
import numpy as np
import jax
import jax.numpy as jnp

def _softmax(x, axis=-1):
    return jax.nn.softmax(x, axis=axis)

def _gelu(x):
    return jax.nn.gelu(x, approximate=True)

def _silu(x):
    return jax.nn.silu(x)

def _sigmoid(x):
    return jax.nn.sigmoid(x)

def _layernorm(x, axis=-1, eps=1e-05):
    m = jnp.mean(x, axis=axis, keepdims=True)
    v = jnp.var(x, axis=axis, keepdims=True)
    return (x - m) / jnp.sqrt(v + eps)

def _scatter_add(tgt, idx, src, axis=0):
    return tgt.at[idx].add(src)

def _segment_sum(src, seg, n):
    return jax.ops.segment_sum(src, seg, n)
kernel_name = 'mk_dlrm_tower_d1_rec_r8_57bd72'

def setup_inputs(seed: int=0):
    np.random.seed(seed)
    _w = jnp.asarray

    def _rec_inputs():
        import jax
        import jax.numpy as jnp
        _tk = jax.random.key(seed)
        ids = jnp.stack([jax.random.randint(jax.random.fold_in(_tk, 200 + f), (2048,), 0, v, jnp.int32) for f, v in enumerate([12500, 1000, 1250, 125000, 1250, 1000, 1000, 1000, 1000, 1000, 1250, 12500, 1250, 12500, 1250, 1000, 1250, 12500, 12500, 1000, 1250, 12500, 1250, 1000, 12500, 12500])], axis=1)
        tbl_0 = 0.05 * jax.random.normal(jax.random.fold_in(_tk, 500 + 0), (12500, 128), jnp.float32)
        tbl_1 = 0.05 * jax.random.normal(jax.random.fold_in(_tk, 500 + 1), (1000, 128), jnp.float32)
        tbl_2 = 0.05 * jax.random.normal(jax.random.fold_in(_tk, 500 + 2), (1250, 128), jnp.float32)
        tbl_3 = 0.05 * jax.random.normal(jax.random.fold_in(_tk, 500 + 3), (125000, 128), jnp.float32)
        tbl_4 = 0.05 * jax.random.normal(jax.random.fold_in(_tk, 500 + 4), (1250, 128), jnp.float32)
        tbl_5 = 0.05 * jax.random.normal(jax.random.fold_in(_tk, 500 + 5), (1000, 128), jnp.float32)
        tbl_6 = 0.05 * jax.random.normal(jax.random.fold_in(_tk, 500 + 6), (1000, 128), jnp.float32)
        tbl_7 = 0.05 * jax.random.normal(jax.random.fold_in(_tk, 500 + 7), (1000, 128), jnp.float32)
        tbl_8 = 0.05 * jax.random.normal(jax.random.fold_in(_tk, 500 + 8), (1000, 128), jnp.float32)
        tbl_9 = 0.05 * jax.random.normal(jax.random.fold_in(_tk, 500 + 9), (1000, 128), jnp.float32)
        tbl_10 = 0.05 * jax.random.normal(jax.random.fold_in(_tk, 500 + 10), (1250, 128), jnp.float32)
        tbl_11 = 0.05 * jax.random.normal(jax.random.fold_in(_tk, 500 + 11), (12500, 128), jnp.float32)
        tbl_12 = 0.05 * jax.random.normal(jax.random.fold_in(_tk, 500 + 12), (1250, 128), jnp.float32)
        tbl_13 = 0.05 * jax.random.normal(jax.random.fold_in(_tk, 500 + 13), (12500, 128), jnp.float32)
        tbl_14 = 0.05 * jax.random.normal(jax.random.fold_in(_tk, 500 + 14), (1250, 128), jnp.float32)
        tbl_15 = 0.05 * jax.random.normal(jax.random.fold_in(_tk, 500 + 15), (1000, 128), jnp.float32)
        tbl_16 = 0.05 * jax.random.normal(jax.random.fold_in(_tk, 500 + 16), (1250, 128), jnp.float32)
        tbl_17 = 0.05 * jax.random.normal(jax.random.fold_in(_tk, 500 + 17), (12500, 128), jnp.float32)
        tbl_18 = 0.05 * jax.random.normal(jax.random.fold_in(_tk, 500 + 18), (12500, 128), jnp.float32)
        tbl_19 = 0.05 * jax.random.normal(jax.random.fold_in(_tk, 500 + 19), (1000, 128), jnp.float32)
        tbl_20 = 0.05 * jax.random.normal(jax.random.fold_in(_tk, 500 + 20), (1250, 128), jnp.float32)
        tbl_21 = 0.05 * jax.random.normal(jax.random.fold_in(_tk, 500 + 21), (12500, 128), jnp.float32)
        tbl_22 = 0.05 * jax.random.normal(jax.random.fold_in(_tk, 500 + 22), (1250, 128), jnp.float32)
        tbl_23 = 0.05 * jax.random.normal(jax.random.fold_in(_tk, 500 + 23), (1000, 128), jnp.float32)
        tbl_24 = 0.05 * jax.random.normal(jax.random.fold_in(_tk, 500 + 24), (12500, 128), jnp.float32)
        tbl_25 = 0.05 * jax.random.normal(jax.random.fold_in(_tk, 500 + 25), (12500, 128), jnp.float32)
        _rk = jax.random.fold_in(_tk, 7)
        r_dense_features = -0.000520686 + 1.00062 * jax.random.normal(jax.random.fold_in(_rk, 101), (2048, 128), jnp.float32)
        W_top1 = 0.0405887 * jax.random.normal(jax.random.fold_in(_tk, 801), (607, 512), jnp.float32)
        W_top2 = 0.0441942 * jax.random.normal(jax.random.fold_in(_tk, 802), (512, 256), jnp.float32)
        W_top3 = 0.0625 * jax.random.normal(jax.random.fold_in(_tk, 803), (256, 1), jnp.float32)
        b_top1 = jnp.zeros((512,), jnp.float32)
        b_top2 = jnp.zeros((256,), jnp.float32)
        return (r_dense_features, ids, tbl_0, tbl_1, tbl_2, tbl_3, tbl_4, tbl_5, tbl_6, tbl_7, tbl_8, tbl_9, tbl_10, tbl_11, tbl_12, tbl_13, tbl_14, tbl_15, tbl_16, tbl_17, tbl_18, tbl_19, tbl_20, tbl_21, tbl_22, tbl_23, tbl_24, tbl_25, W_top1, b_top1, W_top2, b_top2, W_top3)
    r_dense_features, ids, tbl_0, tbl_1, tbl_2, tbl_3, tbl_4, tbl_5, tbl_6, tbl_7, tbl_8, tbl_9, tbl_10, tbl_11, tbl_12, tbl_13, tbl_14, tbl_15, tbl_16, tbl_17, tbl_18, tbl_19, tbl_20, tbl_21, tbl_22, tbl_23, tbl_24, tbl_25, W_top1, b_top1, W_top2, b_top2, W_top3 = _rec_inputs()

    def _L0_rec_setup():
        import jax, jax.numpy as jnp
        import numpy as np
        F = 26
        N = F + 1
        _TRIU_I, _TRIU_J = np.triu_indices(N, k=1)
        key = jax.random.key(seed)
        k1, k2 = jax.random.split(key)
        B, D = (2048, 128)
        dense_features = jax.random.normal(k1, (B, D), dtype=jnp.float32)
        sparse_features = jax.random.normal(k2, (B, F, D), dtype=jnp.float32)
        return {'dense_features': dense_features, 'sparse_features': sparse_features}
    _L0_rec_all = _L0_rec_setup()
    _L0_rec_in = {k: v for k, v in _L0_rec_all.items() if k in ()}
    del _L0_rec_all
    return {'r_dense_features': r_dense_features, 'ids': ids, 'tbl_0': tbl_0, 'tbl_1': tbl_1, 'tbl_2': tbl_2, 'tbl_3': tbl_3, 'tbl_4': tbl_4, 'tbl_5': tbl_5, 'tbl_6': tbl_6, 'tbl_7': tbl_7, 'tbl_8': tbl_8, 'tbl_9': tbl_9, 'tbl_10': tbl_10, 'tbl_11': tbl_11, 'tbl_12': tbl_12, 'tbl_13': tbl_13, 'tbl_14': tbl_14, 'tbl_15': tbl_15, 'tbl_16': tbl_16, 'tbl_17': tbl_17, 'tbl_18': tbl_18, 'tbl_19': tbl_19, 'tbl_20': tbl_20, 'tbl_21': tbl_21, 'tbl_22': tbl_22, 'tbl_23': tbl_23, 'tbl_24': tbl_24, 'tbl_25': tbl_25, 'W_top1': W_top1, 'b_top1': b_top1, 'W_top2': W_top2, 'b_top2': b_top2, 'W_top3': W_top3}

def reference(r_dense_features, ids, tbl_0, tbl_1, tbl_2, tbl_3, tbl_4, tbl_5, tbl_6, tbl_7, tbl_8, tbl_9, tbl_10, tbl_11, tbl_12, tbl_13, tbl_14, tbl_15, tbl_16, tbl_17, tbl_18, tbl_19, tbl_20, tbl_21, tbl_22, tbl_23, tbl_24, tbl_25, W_top1, b_top1, W_top2, b_top2, W_top3):
    import jax
    import jax.numpy as jnp

    def _L0_rec_ref(dense_features, sparse_features):
        import jax, jax.numpy as jnp
        import numpy as np
        F = 26
        N = F + 1
        _TRIU_I, _TRIU_J = np.triu_indices(N, k=1)
        combined = jnp.concatenate([dense_features[:, None, :], sparse_features], axis=1)
        interactions = jnp.einsum('bnd,bmd->bnm', combined, combined)
        interactions_flat = interactions[:, _TRIU_I, _TRIU_J]
        return jnp.concatenate([dense_features, interactions_flat], axis=1)
    e = jnp.stack([tbl_0[ids[:, 0]], tbl_1[ids[:, 1]], tbl_2[ids[:, 2]], tbl_3[ids[:, 3]], tbl_4[ids[:, 4]], tbl_5[ids[:, 5]], tbl_6[ids[:, 6]], tbl_7[ids[:, 7]], tbl_8[ids[:, 8]], tbl_9[ids[:, 9]], tbl_10[ids[:, 10]], tbl_11[ids[:, 11]], tbl_12[ids[:, 12]], tbl_13[ids[:, 13]], tbl_14[ids[:, 14]], tbl_15[ids[:, 15]], tbl_16[ids[:, 16]], tbl_17[ids[:, 17]], tbl_18[ids[:, 18]], tbl_19[ids[:, 19]], tbl_20[ids[:, 20]], tbl_21[ids[:, 21]], tbl_22[ids[:, 22]], tbl_23[ids[:, 23]], tbl_24[ids[:, 24]], tbl_25[ids[:, 25]]], axis=1)
    z = _L0_rec_ref(r_dense_features, e)
    z = z.reshape(z.shape[0], -1)
    h = jnp.concatenate([z, r_dense_features], axis=1)
    h = jnp.maximum(h @ W_top1 + b_top1, 0.0)
    h = jnp.maximum(h @ W_top2 + b_top2, 0.0)
    y = h @ W_top3
    return y

_drawn_inputs = setup_inputs


def setup_inputs(seed=0):
    import zlib

    import numpy as np

    out = dict(_drawn_inputs(seed))
    spreads = {'b_top1': (0.0, 0.1), 'b_top2': (0.0, 0.1)}
    factors = {}
    for name, (base, spread) in spreads.items():
        noise = np.random.default_rng([zlib.crc32(name.encode()), seed]).standard_normal(out[name].shape)
        drawn = base * np.exp(spread * noise) if base else spread * noise
        out[name] = jnp.asarray(drawn.astype(out[name].dtype))
    for name, factor in factors.items():
        out[name] = (out[name] * factor).astype(out[name].dtype)
    return out
```

```python
import numpy as np
import concourse.bass as bass
from concourse import mybir
from contextlib import ExitStack

FIELDS = 26
FEATS = FIELDS + 1
PAD = 32
QUADS = 128 // PAD


def pair_slots():
    h = FEATS // 2
    q = (h + 1) // 2
    copies, slot = [], 0

    def add(j0, i0, dims):
        nonlocal slot
        copies.append((slot, j0, i0, dims))
        slot += int(np.prod([n for _, _, n in dims]))

    add(0, h + 1, ((1, 0, h), (0, 1, FEATS - h - 1)))
    add(0, q, ((h, h, 2), (1, 0, q), (0, 1, q)))
    for c in (0, h):
        add(c, c + 1, ((q, q, 2), (1, 1, q - 1), (0, 1, 3)))
        add(c, c + 4, ((q, q, 2), (1, 0, 3), (0, 1, 3)))
    table = []
    for _, j0, i0, dims in copies:
        for at in np.ndindex(*[n for _, _, n in dims]):
            j = j0 + sum(a * d[0] for a, d in zip(at, dims))
            i = i0 + sum(a * d[1] for a, d in zip(at, dims))
            table.append((j, i))
    seen, slots = set(), []
    for j, i in table:
        fresh = j < i < FEATS and (j, i) not in seen
        seen.add((j, i))
        slots.append((j, i) if fresh else None)
    assert sum(s is not None for s in slots) == FEATS * (FEATS - 1) // 2
    return copies, slots


STEPS_OF = {
    "h": lambda w: ("hot", int(w[1:])), "s": lambda w: ("small", int(w[1:])),
    "a": lambda w: ("turn", 0, int(w[1:])), "b": lambda w: ("turn", 1, int(w[1:])),
    "A": lambda w: ("gram", 0, int(w[1:])), "B": lambda w: ("gram", 1, int(w[1:])),
    "P": lambda w: ("pack", int(w[1:])),
    "o": lambda w: ("build", int(w[1]), int(w[2])), "n": lambda w: ("ahead", int(w[1]), int(w[2])),
}
TENSOR_STEPS = """
    h0 h1 h2 s0 h3 a0 h4 a1 h5 a2 s1 h6 a3 s2 a4 s3 A0 A1 A2 A3 s4 A4
    b0 A5 A6 A7 s5 b1 s6 b2 s7 b3 b4 s8 B0 B1 B2 B3 B4 B5 B6 B7"""
SCALAR_STEPS = """
    h0 h1 o40 o41 h2 s0 h3 a0 h4 a1 h5 a2 s1 h6 a3 s2 a4 s3 A0 A1 A2 A3
    s4 A4 b0 A5 A6 A7 s5 b1 s6 b2 s7 b3 b4 s8 B0 B1 B2 B3 B4 B5 B6 B7"""
VECTOR_STEPS = """
    o30 o31 P1 o50 a0 o51 o60 a1 o61 a2 a3 a4 A0 A1 A2 A3 n00 A4 n01 b0 A5 A6
    A7 P0 n10 b1 n11 b2 b3 b4 B0 B1 n20 B2 B3 B4 n21 B5 B6 B7"""


def last_order(steps, tile_steps):
    at = steps.index(("turn", 1, 0))
    early = [s for s in steps[at:] if s[0] not in ("turn", "gram", "pack") or s[1] == 0]
    return (steps[:at] + early + [("layers", 0, k) for k in range(tile_steps)]
            + [s for s in steps[at:] if s not in early] + [("layers", 1, k) for k in range(tile_steps)])


COPIES, SLOTS = pair_slots()
ROW_CHUNKS = 8
HOT = 7

PAIR_CHUNKS = -(-len(SLOTS) // 128)


def split_fields(rows):
    fit = [f for f in range(FIELDS) if rows[f] % ROW_CHUNKS == 0 and rows[f] <= 128 * ROW_CHUNKS]
    hot = [f for f in fit if rows[f] == rows[fit[0]]][:HOT]
    return hot, [f for f in range(FIELDS) if f not in hot]


def dlrm_tower(nc, x, ids, hot_ids, tables, hot_tables, wz, w1, b1, w2, b2, w3, out):
    f32 = mybir.dt.float32
    f32r = mybir.dt.float32r
    i32 = mybir.dt.int32
    ACT = mybir.ActivationFunctionType
    ALU = mybir.AluOpType

    B, D = x.shape
    H1, H2 = w2.shape
    NPAIR = FEATS * (FEATS - 1) // 2
    NHOT = len(hot_tables)
    NG = FEATS - NHOT
    HROWS = hot_tables[0].shape[0] // ROW_CHUNKS
    TB = 128
    PB = 2 * TB
    PAIRS = B // PB
    GROUPS = TB // QUADS
    FW = FEATS + FEATS % 2
    TQ = -(-NG // 4)
    UG = 4
    TU = GROUPS // UG
    N1, N2 = H1 // 128, H2 // 128
    SU = 2 + N1 + N2 + 1
    SL = SU - 1
    DVE_UNITS = (1, 4, 7)
    IROWS = FEATS + 2
    RING = 3

    SCHEDULE, ACT_ORDER, DVE_ORDER = (
        [STEPS_OF[word[0]](word) for word in order.split()] for order in (TENSOR_STEPS, SCALAR_STEPS, VECTOR_STEPS))
    hots = [("hot", n) for n in range(NHOT)]
    turns = [[("turn", t, c) for c in range(TQ)] for t in range(2)]
    assert ([x for x in SCHEDULE if x[0] == "hot"], [x for x in SCHEDULE if x[0] == "turn"]) == (hots, turns[0] + turns[1])
    assert [x for x in ACT_ORDER if x[0] not in ("build", "ahead")] == SCHEDULE
    BUILDER = {x[1]: engine for engine, order in (("act", ACT_ORDER), ("dve", DVE_ORDER))
               for x in order if x[0] in ("build", "ahead")}
    BUILT = {engine: sorted(n for n in BUILDER if BUILDER[n] == engine) for engine in ("act", "dve")}
    assert sorted(BUILDER) == list(range(NHOT))
    USES = [x for x in SCHEDULE if x[0] in ("hot", "turn")]
    FU = len(USES)
    USE = {x: u for u, x in enumerate(USES)}

    ctx = ExitStack()
    with ctx:
        def sb(name, shape, dt=f32):
            return ctx.enter_context(nc.sbuf_tensor(name, shape, dt))

        def pb(name, shape):
            return ctx.enter_context(nc.psum_tensor(name, shape, f32))

        def sem(name):
            return ctx.enter_context(nc.semaphore(name))

        idx = sb("idx", [TB, 2, NG - 1], i32)
        emb = sb("emb", [TB, 2, NG, D])
        embT = sb("embT", [D, 2, 2, GROUPS, QUADS, PAD], f32r)
        tab = sb("tab", [HROWS, NHOT, 2, ROW_CHUNKS, D], f32r)
        want = sb("want", [HROWS, NHOT, PB], i32)
        row0 = sb("row0", [HROWS, 1])
        minus_row = sb("minus_row", [HROWS, ROW_CHUNKS])
        onehot = sb("onehot", [HROWS, RING, ROW_CHUNKS, PB], f32r)
        xT = sb("xT", [D, 2 * PB])
        gram = sb("gram", [128, 2, FEATS, GROUPS])
        inter = sb("inter", [TB, IROWS * PAD])
        packed = sb("packed", [TB, PAIR_CHUNKS * 128])
        packT = sb("packT", [128, PAIR_CHUNKS, PB])
        h1 = sb("h1", [128, N1, PB])
        h2 = sb("h2", [128, N2, PB])
        y = sb("y", [1, PB])
        ident = sb("ident", [128, 128])
        wz_sb = sb("wz_sb", [128, PAIR_CHUNKS, H1])
        wx_sb = sb("wx_sb", [D, H1])
        w2_sb = sb("w2_sb", [128, N1, H2])
        w3_sb = sb("w3_sb", [128, N2])
        b1_sb = sb("b1_sb", [128, N1])
        b2_sb = sb("b2_sb", [128, N2])
        raw = [gram[0:HROWS].rearrange("p t j g -> p (t j g)")[:, 0:ROW_CHUNKS * D],
               h1[0:HROWS].rearrange("p n b -> p (n b)"),
               wz_sb[0:HROWS].rearrange("p c n -> p (c n)")[:, 0:ROW_CHUNKS * D],
               w2_sb[0:HROWS].rearrange("p c n -> p (c n)")]
        RAW = len(raw)
        wx2 = packT[:].rearrange("p c b -> p (c b)")[:, 0:H1]

        pF = pb("pF", [128, 2, 512])
        pG = pb("pG", [128, 2, UG, 256])
        pM = pb("pM", [128, 2, 512])

        consts = sem("consts")
        raw_in = [sem(f"raw_in{r}") for r in range(RAW)]
        tab_high = sem("tab_high")
        tab_done = sem("tab_done")
        weights_in = sem("weights_in")
        wx_added = sem("wx_added")
        idx_in = [sem("idx_in0"), sem("idx_in1")]
        want_in = sem("want_in")
        gathered = [sem("gathered0"), sem("gathered1")]
        dense_in = [sem("dense_in0"), sem("dense_in1")]
        columns_act = sem("columns_act")
        columns_dve = sem("columns_dve")
        distances = sem("distances")
        feat_done = sem("feat_done")
        feat_high = sem("feat_high")
        feat_low = sem("feat_low")
        gram_done = sem("gram_done")
        gram_act = sem("gram_act")
        gram_dve = sem("gram_dve")
        halves_added = sem("halves_added")
        inter_done = sem("inter_done")
        packed_done = sem("packed_done")
        small_done = sem("small_done")
        small_read = sem("small_read")
        stored = sem("stored")
        NW = 7

        CUT = tuple(USE[turns[t][-1]] + 1 for t in range(2))
        assert CUT[0] > USE[hots[-1]] and CUT[1] == FU
        LOW = [sum(x[0] == "turn" for x in USES[:v + 1]) for v in range(FU)]

        dve_units = [n for n in range(2 * TU) if n % TU in DVE_UNITS]
        act_units = [n for n in range(2 * TU) if n % TU not in DVE_UNITS]

        def wait_unit_read(eng, p, n):
            if n in dve_units:
                eng.wait_ge(gram_dve, p * len(dve_units) + dve_units.index(n) + 1)
            else:
                eng.wait_ge(gram_act, p * len(act_units) + act_units.index(n) + 1)

        def read_unit(eng, copy, p, t, u, first, done):
            n = t * TU + u
            if u in (min(DVE_UNITS), 0) and (t or not first):
                eng.wait_ge(inter_done, p * 2 + t)
            eng.wait_ge(gram_done, p * (2 * TU) + n + 1)
            for a in range(QUADS):
                rows = slice(a * PAD, a * PAD + PAD)
                part = pG[rows, n % 2, :, 0:2 * QUADS * FW].rearrange("p g (l q j) -> p l g q j", l=2, q=QUADS)
                dst = gram[rows, :, :, UG * u:UG * u + UG].rearrange("p l j g -> p l g j")
                last = copy(dst, part[:, :, :, a, 0:FEATS])
            last.then_inc(done, 1)

        def wait_built(eng, p, n):
            mine = BUILT[BUILDER[n]]
            eng.wait_ge(columns_act if BUILDER[n] == "act" else columns_dve, p * len(mine) + mine.index(n) + 1)

        def wait_columns_free(eng, p, n, very_first):
            eng.wait_ge(want_in, p * 16 + 16)
            if n >= RING:
                eng.wait_ge(feat_done, p * FU + USE["hot", n - RING] + 1)
            elif not very_first:
                v = max(m for m in range(NHOT) if (m - n) % RING == 0)
                eng.wait_ge(feat_done, (p - 1) * FU + USE["hot", v] + 1)

        block = ctx.enter_context(nc.Block())

        @block.sync
        def _(sp):
            def load_idx(p, t):
                sp.dma_start(idx[:, t, :], ids[bass.ds(p * PB + t * TB, TB), :]).then_inc(idx_in[t], 16)

            def load_dense(p, t):
                sp.dma_start(emb[:, t, 0, :], x[bass.ds(p * PB + t * TB, TB), :]).then_inc(dense_in[t], 16)

            for t in range(2):
                load_idx(0, t)
            for n in range(NHOT):
                if n >= RAW:
                    sp.wait_ge(tab_done, 2 + n - RAW + 1)
                sp.dma_start(raw[n % RAW].rearrange("p (c d) -> p c d", d=D),
                             hot_tables[n].rearrange("(p c) d -> p c d", c=ROW_CHUNKS)).then_inc(raw_in[n % RAW], 16)
                if n == 1:
                    for t in range(2):
                        load_dense(0, t)
            sp.wait_ge(tab_done, 2 + NHOT)
            sp.dma_start(wz_sb[:], wz.rearrange("(c p) n -> p c n", p=128)).then_inc(weights_in, 16)
            sp.dma_start(wx_sb[:], w1[0:D, :]).then_inc(weights_in, 16)
            sp.dma_start(wx2, w1[D + NPAIR:D + NPAIR + D, :]).then_inc(weights_in, 16)
            sp.dma_start(w2_sb[:], w2.rearrange("(c p) n -> p c n", p=128)).then_inc(weights_in, 16)
            sp.dma_start(w3_sb[:], w3[:, :]).then_inc(weights_in, 16)
            sp.dma_start(b1_sb[:], b1[:, :]).then_inc(weights_in, 16)
            sp.dma_start(b2_sb[:], b2[:, :]).then_inc(weights_in, 16)
            with sp.Fori(1, PAIRS) as p:
                sp.wait_ge(gathered[0], p * (16 * (NG - 1)))
                load_idx(p, 0)
                sp.wait_ge(feat_done, p * FU + (CUT[0] - FU))
                load_dense(p, 0)
                sp.wait_ge(gathered[1], p * (16 * (NG - 1)))
                load_idx(p, 1)
                sp.wait_ge(feat_done, p * FU)
                load_dense(p, 1)

        @block.gpsimd
        def _(pool):
            def gather(t):
                for f in range(NG - 1):
                    pool.indirect_dma_start(
                        out=emb[:, t, 1 + f, :], out_offset=None, in_=tables[f][:, :],
                        in_offset=bass.IndirectOffsetOnAxis(ap=idx[:, t, f:f + 1], axis=0),
                    ).then_inc(gathered[t], 16)

            pool.iota(row0[:], [[0, 1]], channel_multiplier=ROW_CHUNKS,
                      allow_small_or_imprecise_dtypes=True).then_inc(consts, 1)
            pool.iota(minus_row[:], [[-1, ROW_CHUNKS]], channel_multiplier=-ROW_CHUNKS,
                      allow_small_or_imprecise_dtypes=True).then_inc(consts, 1)
            pool.memset(ident[:], 0.0).then_inc(consts, 1)
            pool.wait_ge(consts, 3)
            pool.affine_select(out=ident[:], in_=ident[:], compare_op=ALU.not_equal, fill=1.0, base=0,
                               pattern=[[-1, 128]], channel_multiplier=1).then_inc(consts, 1)
            emb_free = pool.alloc_register("emb_free")
            pool.reg_mov(emb_free, CUT[0])
            for t in range(2):
                pool.wait_ge(idx_in[t], 16)
                gather(t)
            with pool.Fori(1, PAIRS) as p:
                for t in range(2):
                    pool.wait_ge(idx_in[t], p * 16 + 16)
                    pool.wait_ge(feat_done, emb_free)
                    pool.reg_add(emb_free, emb_free, FU - CUT[0] if t == 0 else CUT[0])
                    gather(t)

        @block.tensor
        def _(pe):
            def wait_feature_bank(p, u, first):
                v = u - 2 if u >= 2 else (FU - 1 if (FU - 1 - u) % 2 == 0 else FU - 2)
                q = p if u >= 2 else p - 1
                if u < 2 and first:
                    return
                if USES[v][0] == "hot":
                    pe.wait_ge(feat_high, q * FU + v + 1)
                else:
                    pe.wait_ge(feat_low, q * (2 * TQ) + LOW[v])

            def look_up(p, n, first):
                u = USE["hot", n]
                if first:
                    pe.wait_ge(tab_done, 2 + n + 1)
                wait_built(pe, p, n)
                wait_feature_bank(p, u, first)
                for part in range(2):
                    for c in range(ROW_CHUNKS):
                        last = pe.matmul(pF[:, u % 2, part * PB:(part + 1) * PB], tab[:, n, part, c, :],
                                         onehot[:, n % RING, c, :], start=(c == 0), stop=(c == ROW_CHUNKS - 1))
                last.then_inc(feat_done, 1)

            def turn(p, t, c, first):
                u = USE["turn", t, c]
                if c == 0:
                    pe.wait_ge(gathered[t], p * (16 * (NG - 1)) + 16 * (NG - 1))
                    pe.wait_ge(dense_in[t], p * 16 + 16)
                wait_feature_bank(p, u, first)
                for f in range(4 * c, min(4 * c + 4, NG)):
                    last = pe.transpose(pF[:, u % 2, (f % 4) * 128:(f % 4) * 128 + 128], emb[:, t, f, :], ident[:])
                last.then_inc(feat_done, 1)

            def gram_unit(p, t, u, first):
                n = t * TU + u
                if u == 0:
                    pe.wait_ge(feat_high, p * FU + CUT[t])
                    pe.wait_ge(feat_low, p * (2 * TQ) + TQ * (t + 1))
                if n >= 2 or not first:
                    wait_unit_read(pe, p if n >= 2 else p - 1, (n - 2) % (2 * TU))
                for g in range(UG):
                    left = embT[:, 0, t, UG * u + g, :, :].rearrange("p q f -> p (q f)")
                    right = embT[:, :, t, UG * u + g, :, 0:FW]
                    last = pe.matmul(pG[:, n % 2, g, 0:2 * QUADS * FW], left, right,
                                     start=(g % 2 == 0), stop=True, skip_group_check=True)
                last.then_inc(gram_done, 1)

            def small(m, k, very_first):
                v = k - 2 if k >= 2 else (SU - 1 if (SU - 1 - k) % 2 == 0 else SU - 2)
                if k >= 2 or not very_first:
                    pe.wait_ge(small_read, (m if k >= 2 else m - 1) * SU + v + 1)
                bank = pM[:, k % 2, 0:PB]
                if k < 2:
                    pe.wait_ge(packed_done, m * 2 + k + 1)
                    for c in range(PAIR_CHUNKS):
                        last = pe.transpose(pM[:, k % 2, c * 128:c * 128 + 128],
                                            packed[:, c * 128:c * 128 + 128], ident[:])
                elif k < 2 + N1:
                    n = k - 2
                    cols = slice(n * 128, n * 128 + 128)
                    pe.wait_ge(small_read, m * SU + 2)
                    pe.matmul(bank, wx_sb[:, cols], xT[:, bass.ds((m % 2) * PB, PB)], start=True, stop=False)
                    for c in range(PAIR_CHUNKS):
                        last = pe.matmul(bank, wz_sb[:, c, cols], packT[:, c, :], start=False,
                                         stop=(c == PAIR_CHUNKS - 1))
                elif k < 2 + N1 + N2:
                    pe.wait_ge(small_read, m * SU + 2 + N1)
                    n = k - 2 - N1
                    for c in range(N1):
                        last = pe.matmul(bank, w2_sb[:, c, n * 128:n * 128 + 128], h1[:, c, :],
                                         start=(c == 0), stop=(c == N1 - 1))
                else:
                    pe.wait_ge(small_read, m * SU + SU - 1)
                    for c in range(N2):
                        last = pe.matmul(bank[0:1, :], w3_sb[:, c:c + 1], h2[:, c, :],
                                         start=(c == 0), stop=(c == N2 - 1))
                last.then_inc(small_done, 1)

            def pair(p, first, second=False, order=SCHEDULE):
                for what, *at in order:
                    if what == "hot":
                        look_up(p, *at, first)
                    elif what == "turn":
                        turn(p, *at, first)
                    elif what == "gram":
                        gram_unit(p, *at, first)
                    elif what == "layers":
                        layers(*at)
                    elif not first:
                        small(p - 1, *at, second)

            def layers(t, k):
                base = (PAIRS - 1) * SU + t * SL
                pe.wait_ge(small_read, base + max(k - 1, 0))
                bank = pM[:, k % 2, 0:TB]
                cols = slice(t * TB, (t + 1) * TB)
                if k == 0:
                    pe.wait_ge(packed_done, (PAIRS - 1) * 2 + t + 1)
                    for c in range(PAIR_CHUNKS):
                        last = pe.transpose(pM[:, k % 2, c * 128:c * 128 + 128],
                                            packed[:, c * 128:c * 128 + 128], ident[:])
                elif k < 1 + N1:
                    n = k - 1
                    w = slice(n * 128, n * 128 + 128)
                    pe.wait_ge(small_read, base + 1)
                    at = ((PAIRS - 1) % 2) * PB + t * TB
                    pe.matmul(bank, wx_sb[:, w], xT[:, at:at + TB], start=True, stop=False)
                    for c in range(PAIR_CHUNKS):
                        last = pe.matmul(bank, wz_sb[:, c, w], packT[:, c, cols], start=False,
                                         stop=(c == PAIR_CHUNKS - 1))
                elif k < 1 + N1 + N2:
                    pe.wait_ge(small_read, base + 1 + N1)
                    n = k - 1 - N1
                    for c in range(N1):
                        last = pe.matmul(bank, w2_sb[:, c, n * 128:n * 128 + 128], h1[:, c, cols],
                                         start=(c == 0), stop=(c == N1 - 1))
                else:
                    pe.wait_ge(small_read, base + SL - 1)
                    for c in range(N2):
                        last = pe.matmul(bank[0:1, :], w3_sb[:, c:c + 1], h2[:, c, cols],
                                         start=(c == 0), stop=(c == N2 - 1))
                last.then_inc(small_done, 1)

            pe.wait_ge(consts, 4)
            pair(0, True)
            pe.wait_ge(weights_in, 16 * NW)
            pe.wait_ge(wx_added, 1)
            pair(1, False, True)
            with pe.Fori(2, PAIRS - 1) as p:
                pair(p, False)
            pair(PAIRS - 1, False, order=last_order(SCHEDULE, SL))

        @block.scalar
        def _(act):
            def copy(dst, src):
                return act.activation(dst, src, ACT.Copy)

            def load_want(p):
                src = hot_ids[:, bass.ds(p * PB, PB)]
                src = bass.AP(src.tensor, src.offset, [[0, HROWS]] + list(src.ap))
                act.dma_start(want[:], src).then_inc(want_in, 16)

            def read_hot(p, n):
                u = USE["hot", n]
                act.wait_ge(feat_done, p * FU + u + 1)
                for part in range(2):
                    last = copy(embT[:, part, :, :, :, NG + n].rearrange("p t g q -> p t q g"),
                                pF[:, u % 2, part * PB:(part + 1) * PB].rearrange("p (t q g) -> p t q g", t=2, q=QUADS))
                last.then_inc(feat_high, 1)

            def read_high(p, t, c):
                u = USE["turn", t, c]
                act.wait_ge(feat_done, p * FU + u + 1)
                n = min(4, NG - 4 * c)
                src = pF[:, u % 2, 0:n * 128].rearrange("p (f b) -> p f b", b=TB)
                if c == 0:
                    copy(xT[:, bass.ds((p % 2) * PB + t * TB, TB)], src[:, 0, :])
                copy(embT[:, 0, t, :, :, 4 * c:4 * c + n].rearrange("p g q f -> p f q g"),
                     src.rearrange("p f (q g) -> p f q g", q=QUADS)).then_inc(feat_high, 1)

            def read_small(m, k, very_first):
                act.wait_ge(small_done, m * SU + k + 1)
                bank = pM[:, k % 2, 0:PB]
                if k < 2:
                    copy(packT[:, :, k * TB:(k + 1) * TB],
                         pM[:, k % 2, 0:PAIR_CHUNKS * 128].rearrange("p (c b) -> p c b", b=TB)).then_inc(small_read, 1)
                elif k < 2 + N1:
                    n = k - 2
                    act.activation(h1[:, n, :], bank, ACT.Relu, bias=b1_sb[:, n:n + 1]).then_inc(small_read, 1)
                elif k < 2 + N1 + N2:
                    n = k - 2 - N1
                    act.activation(h2[:, n, :], bank, ACT.Relu, bias=b2_sb[:, n:n + 1]).then_inc(small_read, 1)
                else:
                    if not very_first:
                        act.wait_ge(stored, m * 16)
                    copy(y[:], bank[0:1, :]).then_inc(small_read, 1)
                    act.wait_ge(small_read, m * SU + SU)
                    act.dma_start(out[bass.ds(m * PB, PB), :].rearrange("b n -> n b"), y[:]).then_inc(stored, 16)

            def read_layers(t, k):
                base = (PAIRS - 1) * SU + t * SL
                act.wait_ge(small_done, base + k + 1)
                bank = pM[:, k % 2, 0:TB]
                cols = slice(t * TB, (t + 1) * TB)
                if k == 0:
                    copy(packT[:, :, cols],
                         pM[:, k % 2, 0:PAIR_CHUNKS * 128].rearrange("p (c b) -> p c b", b=TB)).then_inc(small_read, 1)
                elif k < 1 + N1:
                    n = k - 1
                    act.activation(h1[:, n, cols], bank, ACT.Relu, bias=b1_sb[:, n:n + 1]).then_inc(small_read, 1)
                elif k < 1 + N1 + N2:
                    n = k - 1 - N1
                    act.activation(h2[:, n, cols], bank, ACT.Relu, bias=b2_sb[:, n:n + 1]).then_inc(small_read, 1)
                else:
                    if t == 0:
                        act.wait_ge(stored, (PAIRS - 1) * 16)
                    copy(y[:, cols], bank[0:1, :]).then_inc(small_read, 1)
                    act.wait_ge(small_read, base + SL)
                    at = (PAIRS - 1) * PB + t * TB
                    act.dma_start(out[at:at + TB, :].rearrange("b n -> n b"), y[:, cols]).then_inc(stored, 16)

            def build(p, n, half, very_first):
                at = [half * ROW_CHUNKS // 2, (half + 1) * ROW_CHUNKS // 2]
                if half == 0:
                    wait_columns_free(act, p, n, very_first)
                for c in range(*at):
                    last = act.activation(onehot[:, n % RING, c, :], want[:, n, :], ACT.Abs,
                                          bias=minus_row[:, c:c + 1])
                last.then_inc(distances, 1)
                act.wait_ge(distances, p * (2 * len(BUILT["act"])) + (2 * BUILT["act"].index(n) + half + 1))
                both = onehot[:, n % RING, at[0]:at[1], :]
                last = act.activation(both, both.bitcast(f32), ACT.Relu, scale=-1.0, bias=1.0)
                if half:
                    last.then_inc(columns_act, 1)

            def pair(p, first, second=False, last=False, order=ACT_ORDER):
                if not first:
                    act.wait_ge(gram_done, p * (2 * TU))
                for what, *at in order:
                    if what == "hot":
                        read_hot(p, *at)
                        if at[0] == NHOT - 2 and not last:
                            wait_built(act, p, BUILT["act"][-1])
                            wait_built(act, p, BUILT["dve"][-1])
                            load_want(p + 1)
                    elif what == "build":
                        build(p, *at, False)
                    elif what == "ahead":
                        if not last:
                            build(p + 1, *at, False)
                    elif what == "turn":
                        read_high(p, *at)
                    elif what == "gram":
                        if at[1] not in DVE_UNITS:
                            read_unit(act, copy, p, *at, first, gram_act)
                    elif what == "layers":
                        read_layers(*at)
                    elif not first:
                        read_small(p - 1, *at, second)

            load_want(0)
            for n in range(NHOT):
                act.wait_ge(raw_in[n % RAW], 16 * (n // RAW + 1))
                copy(tab[:, n, 0, :, :].rearrange("p c d -> p (c d)"), raw[n % RAW]).then_inc(tab_high, 1)
            act.wait_ge(consts, 4)
            act.wait_ge(tab_done, NHOT + 2)
            pair(0, True)
            act.wait_ge(weights_in, 16 * NW)
            act.wait_ge(wx_added, 1)
            pair(1, False, True)
            with act.Fori(2, PAIRS - 1) as p:
                pair(p, False)
            pair(PAIRS - 1, False, False, True, order=last_order(ACT_ORDER, SL))
            act.wait_ge(stored, 16 * (PAIRS + 1))

        @block.vector
        def _(dve):
            def build(p, n, half, very_first):
                if half == 0:
                    wait_columns_free(dve, p, n, very_first)
                for c in range(half * ROW_CHUNKS // 2, (half + 1) * ROW_CHUNKS // 2):
                    last = dve.tensor_scalar(onehot[:, n % RING, c, :], want[:, n, :], float(c), row0[:, 0:1],
                                             ALU.subtract, ALU.is_equal)
                if half:
                    last.then_inc(columns_dve, 1)

            def read_low(p, t, c):
                u = USE["turn", t, c]
                dve.wait_ge(feat_high, p * FU + u + 1)
                n = min(4, NG - 4 * c)
                src = pF[:, u % 2, 0:n * 128].rearrange("p (f q g) -> p f q g", f=n, q=QUADS)
                high, low = (embT[:, part, t, :, :, 4 * c:4 * c + n].rearrange("p g q f -> p f q g")
                             for part in range(2))
                dve.tensor_tensor(low, src, high.bitcast(f32), ALU.subtract).then_inc(feat_low, 1)

            def pack(p, t, first):
                dve.wait_ge(gram_act, p * len(act_units) + (len(act_units) // 2) * (t + 1))
                dve.wait_ge(gram_dve, p * len(dve_units) + (len(dve_units) // 2) * (t + 1))
                dve.scalar_tensor_tensor(out=gram[:, 1, :, :], in0=gram[:, 0, :, :], scalar=0.5, in1=gram[:, 1, :, :],
                                         op0=ALU.mult, op1=ALU.add).then_inc(halves_added, 1)
                dve.wait_ge(halves_added, p * 2 + t + 1)
                if t or not first:
                    dve.wait_ge(packed_done, p * 2 + t)
                dve.transpose(inter[:, 0:FEATS * PAD], gram[:, 1, :, :]).then_inc(inter_done, 1)
                dve.wait_ge(inter_done, p * 2 + t + 1)
                if t:
                    dve.wait_ge(small_done, p * SU + 1)
                elif not first:
                    dve.wait_ge(small_done, (p - 1) * SU + 2)
                for slot, j0, i0, dims in COPIES:
                    n = [d[2] for d in dims]
                    src = inter[:, :]
                    ji = bass.AP(src.tensor, src.offset + j0 * PAD + i0,
                                 [src.ap[0]] + [[dj * PAD + di, m] for dj, di, m in dims])
                    ij = bass.AP(src.tensor, src.offset + i0 * PAD + j0,
                                 [src.ap[0]] + [[di * PAD + dj, m] for dj, di, m in dims])
                    dst = packed[:, slot:slot + int(np.prod(n))]
                    names = "abc"[:len(n)]
                    dst = dst.rearrange(f"p ({' '.join(names)}) -> p {' '.join(names)}", **dict(zip(names, n)))
                    last = dve.tensor_add(dst, ji, ij)
                last.then_inc(packed_done, 1)

            def pair(p, first, last, order=DVE_ORDER):
                for what, *at in order:
                    if what == "build":
                        build(p, *at, False)
                    elif what == "ahead":
                        if not last:
                            build(p + 1, *at, False)
                    elif what == "turn":
                        read_low(p, *at)
                    elif what == "gram":
                        if at[1] in DVE_UNITS:
                            read_unit(dve, dve.tensor_copy, p, *at, first, gram_dve)
                    elif what == "pack" and at[0] == 0:
                        pack(p, 0, first)
                    elif what == "pack" and not first:
                        pack(p - 1, 1, False)

            dve.memset(embT[:, :, :, :, :, FEATS:PAD].rearrange("p l t g q f -> p (l t g q) f").bitcast(f32), 0.0).then_inc(tab_done, 1)
            dve.memset(packed[:, len(SLOTS):], 0.0)
            dve.memset(inter[:, FEATS * PAD:], 0.0).then_inc(tab_done, 1)
            for n in range(NHOT):
                dve.wait_ge(tab_high, n + 1)
                dve.tensor_tensor(tab[:, n, 1, :, :].rearrange("p c d -> p (c d)"), raw[n % RAW],
                                  tab[:, n, 0, :, :].rearrange("p c d -> p (c d)").bitcast(f32),
                                  ALU.subtract).then_inc(tab_done, 1)
                if n == 0:
                    dve.wait_ge(consts, 4)
                if n < RING:
                    build(0, n, 0, True)
                    build(0, n, 1, True)
            pair(0, True, False)
            dve.wait_ge(weights_in, 16 * NW)
            dve.tensor_add(wx_sb[:], wx_sb[:], wx2).then_inc(wx_added, 1)
            with dve.Fori(1, PAIRS - 1) as p:
                pair(p, False, False)
            pair(PAIRS - 1, False, True, order=last_order(DVE_ORDER, 0))
            pack(PAIRS - 1, 1, False)


def kernel(**inputs):
    import concourse.bacc as bacc
    from concourse.bass_utils import run_bass_kernel_spmd

    a = {k: np.asarray(v) for k, v in inputs.items()}
    w1 = a["W_top1"]
    D = a["r_dense_features"].shape[1]
    hot, cold = split_fields([a[f"tbl_{f}"].shape[0] for f in range(FIELDS)])
    order = [0] + [1 + f for f in cold + hot]
    wz = np.zeros((PAIR_CHUNKS * 128, w1.shape[1]), w1.dtype)
    for slot, pair in enumerate(SLOTS):
        if pair is not None:
            j, i = sorted(order[f] for f in pair)
            wz[slot] = w1[D + j * FEATS - j * (j + 1) // 2 + i - j - 1]

    def by_partition(v):
        return v.reshape(-1, 128).T

    arrays = {"x": a["r_dense_features"], "ids": a["ids"][:, cold], "hot_ids": a["ids"][:, hot].T}
    for f in cold + hot:
        arrays[f"tbl_{f}"] = a[f"tbl_{f}"]
    arrays.update(wz=wz, w1=w1, b1=by_partition(a["b_top1"]), w2=a["W_top2"], b2=by_partition(a["b_top2"]),
                  w3=by_partition(a["W_top3"]))
    arrays = {k: np.ascontiguousarray(v) for k, v in arrays.items()}
    nc = bacc.Bacc("TRN2", target_bir_lowering=False, num_devices=1)
    aps = {k: nc.dram_tensor(f"in_{k}", v.shape, mybir.dt.from_np(v.dtype), kind="ExternalInput").ap()
           for k, v in arrays.items()}
    out = nc.dram_tensor("out_y", (a["ids"].shape[0], 1), mybir.dt.float32, kind="ExternalOutput").ap()
    dlrm_tower(nc, aps["x"], aps["ids"], aps["hot_ids"], [aps[f"tbl_{f}"] for f in cold],
               [aps[f"tbl_{f}"] for f in hot], aps["wz"], aps["w1"], aps["b1"], aps["w2"], aps["b2"],
               aps["w3"], out)
    r = run_bass_kernel_spmd(nc, [{f"in_{k}": v for k, v in arrays.items()}], core_ids=[0])
    return r.results[0]["out_y"]
```

```python
import numpy as np
import concourse.bass as bass
from concourse import mybir
from contextlib import ExitStack

FIELDS = 26
FEATS = FIELDS + 1
PAD = 32
QUADS = 128 // PAD


def pair_slots():
    h = FEATS // 2
    q = (h + 1) // 2
    copies, slot = [], 0

    def add(j0, i0, dims):
        nonlocal slot
        copies.append((slot, j0, i0, dims))
        slot += int(np.prod([n for _, _, n in dims]))

    add(0, h + 1, ((1, 0, h), (0, 1, FEATS - h - 1)))
    add(0, q, ((h, h, 2), (1, 0, q), (0, 1, q)))
    for c in (0, h):
        add(c, c + 1, ((q, q, 2), (1, 1, q - 1), (0, 1, 3)))
        add(c, c + 4, ((q, q, 2), (1, 0, 3), (0, 1, 3)))
    table = []
    for _, j0, i0, dims in copies:
        for at in np.ndindex(*[n for _, _, n in dims]):
            j = j0 + sum(a * d[0] for a, d in zip(at, dims))
            i = i0 + sum(a * d[1] for a, d in zip(at, dims))
            table.append((j, i))
    seen, slots = set(), []
    for j, i in table:
        fresh = j < i < FEATS and (j, i) not in seen
        seen.add((j, i))
        slots.append((j, i) if fresh else None)
    assert sum(s is not None for s in slots) == FEATS * (FEATS - 1) // 2
    return copies, slots


STEPS_OF = {
    "h": lambda w: ("hot", int(w[1:])), "s": lambda w: ("small", int(w[1:])),
    "t": lambda w: ("begin", int(w[1:])),
    "a": lambda w: ("turn", 0, int(w[1:])), "b": lambda w: ("turn", 1, int(w[1:])),
    "A": lambda w: ("gram", 0, int(w[1:])), "B": lambda w: ("gram", 1, int(w[1:])),
    "P": lambda w: ("pack", int(w[1:])), "w": lambda w: ("want", 0),
    "l": lambda w: ("layers", 0, int(w[1:])), "m": lambda w: ("layers", 1, int(w[1:])),
    "o": lambda w: ("build", int(w[1]), int(w[2])), "n": lambda w: ("ahead", int(w[1]), int(w[2])),
}
STEPS = """
    s0 h0 h1 h2 h3 w0 h4 a0 s1 h5 a1 t2 a2 s2 a3 t3 a4 s3 a5 t4 A0 A1
    A2 A3 s4 A4 A5 A6 A7 b0 b1 t5 s5 b2 t6 s6 b3 b4 t7 b5 s7 B0 B1 s8
    B2 B3 B4 B5 B6 B7"""
LAST_STEPS = """
    h0 h1 s0 h2 s1 h3 h4 a0 h5 a1 t2 a2 s2 a3 t3 a4 s3 a5 t4 A0 A1 s4
    A2 A3 A4 A5 s5 A6 A7 s6 b0 b1 b2 s7 b3 s8 l0 b4 b5 l1 l2 B0 B1 l3
    B2 B3 l4 B4 B5 l5 B6 B7 l6 l7 m0 m1 m2 m3 m4 m5 m6 m7"""
VECTOR_STEPS = """
    P1 o40 o41 o50 o51 a0 a1 a2 a3 n00 a4 a5 n01 A0 A1 A2 A3 n10 A4 A5 A6 A7
    n11 b0 b1 P0 b2 b3 n20 n21 b4 b5 n30 B0 n31 B1 B2 B3 B4 B5 B6 B7"""


COPIES, SLOTS = pair_slots()
ROW_CHUNKS = 8
HOT = 6

PAIR_CHUNKS = -(-len(SLOTS) // 128)


def split_fields(rows):
    fit = [f for f in range(FIELDS) if rows[f] % ROW_CHUNKS == 0 and rows[f] <= 128 * ROW_CHUNKS]
    hot = [f for f in fit if rows[f] == rows[fit[0]]][:HOT]
    return hot, [f for f in range(FIELDS) if f not in hot]


def dlrm_tower(nc, x, ids, hot_ids, tables, hot_tables, wz, w1, b1, w2, b2, w3, out):
    f32 = mybir.dt.float32
    f32r = mybir.dt.float32r
    i32 = mybir.dt.int32
    ACT = mybir.ActivationFunctionType
    ALU = mybir.AluOpType

    B, D = x.shape
    H1, H2 = w2.shape
    NPAIR = FEATS * (FEATS - 1) // 2
    NHOT = len(hot_tables)
    NG = FEATS - NHOT
    HROWS = hot_tables[0].shape[0] // ROW_CHUNKS
    TB = 128
    PB = 2 * TB
    PAIRS = B // PB
    GROUPS = TB // QUADS
    FW = FEATS + FEATS % 2
    TQ = -(-NG // 4)
    UG = 4
    TU = GROUPS // UG
    N1, N2 = H1 // 128, H2 // 128
    SU = 2 + N1 + N2 + 1
    SL = SU - 1
    DVE_QUADS = (1, 2, 1, 2, 2, 2, 1, 2)
    IROWS = FEATS + 2
    RING = 4

    ACT_ORDER, ACT_LAST, DVE_ORDER = (
        [STEPS_OF[word[0]](word) for word in order.split()] for order in (STEPS, LAST_STEPS, VECTOR_STEPS))
    SCHEDULE, PE_LAST = (
        [x for x in order if x[0] not in ("build", "ahead", "want")] for order in (ACT_ORDER, ACT_LAST))
    ACT_ORDER, ACT_LAST = ([x for x in order if x[0] != "begin"] for order in (ACT_ORDER, ACT_LAST))
    ACT_FIRST = [x for x in ACT_ORDER if x[0] != "want"]
    ACT_FIRST.insert(ACT_FIRST.index(("hot", NHOT - 1)), ("want", 0))
    hots = [("hot", n) for n in range(NHOT)]
    turns = [[("turn", t, c) for c in range(TQ)] for t in range(2)]
    assert ([x for x in SCHEDULE if x[0] == "hot"], [x for x in SCHEDULE if x[0] == "turn"]) == (hots, turns[0] + turns[1])
    BUILDER = {x[1]: engine for engine, order in (("act", ACT_ORDER), ("dve", DVE_ORDER))
               for x in order if x[0] in ("build", "ahead")}
    BUILT = {engine: sorted(n for n in BUILDER if BUILDER[n] == engine) for engine in ("act", "dve")}
    assert sorted(BUILDER) == list(range(NHOT))
    USES = [x for x in SCHEDULE if x[0] in ("hot", "turn")]
    FU = len(USES)
    assert [x for x in PE_LAST if x[0] in ("hot", "turn")] == USES
    USE = {x: u for u, x in enumerate(USES)}

    ctx = ExitStack()
    with ctx:
        def sb(name, shape, dt=f32):
            return ctx.enter_context(nc.sbuf_tensor(name, shape, dt))

        def pb(name, shape):
            return ctx.enter_context(nc.psum_tensor(name, shape, f32))

        def sem(name):
            return ctx.enter_context(nc.semaphore(name))

        idx = sb("idx", [TB, 2, NG - 1], i32)
        emb = sb("emb", [TB, 2, NG, D])
        embT = sb("embT", [D, 2, 2, GROUPS, QUADS, PAD], f32r)
        tab = sb("tab", [HROWS, NHOT, 2, ROW_CHUNKS, D], f32r)
        want = sb("want", [HROWS, NHOT, PB], i32)
        row0 = sb("row0", [HROWS, 1])
        minus_row = sb("minus_row", [HROWS, ROW_CHUNKS])
        onehot = sb("onehot", [HROWS, RING, ROW_CHUNKS, PB], f32r)
        xT = sb("xT", [D, 2 * PB])
        gram = sb("gram", [128, 2, FEATS, GROUPS])
        inter = sb("inter", [TB, IROWS * PAD])
        packed = sb("packed", [TB, PAIR_CHUNKS * 128])
        packT = sb("packT", [128, PAIR_CHUNKS, PB])
        h1 = sb("h1", [128, N1, PB])
        h2 = sb("h2", [128, N2, PB])
        y = sb("y", [1, PB])
        ident = sb("ident", [128, 128])
        wz_sb = sb("wz_sb", [128, PAIR_CHUNKS, H1])
        wx_sb = sb("wx_sb", [D, H1])
        w2_sb = sb("w2_sb", [128, N1, H2])
        w3_sb = sb("w3_sb", [128, N2])
        b1_sb = sb("b1_sb", [128, N1])
        b2_sb = sb("b2_sb", [128, N2])
        raw = [gram[0:HROWS].rearrange("p t j g -> p (t j g)")[:, 0:ROW_CHUNKS * D],
               h1[0:HROWS].rearrange("p n b -> p (n b)"),
               wz_sb[0:HROWS].rearrange("p c n -> p (c n)")[:, 0:ROW_CHUNKS * D],
               w2_sb[0:HROWS].rearrange("p c n -> p (c n)")]
        RAW = len(raw)
        wx2 = packT[:].rearrange("p c b -> p (c b)")[:, 0:H1]

        pF = pb("pF", [128, 2, 512])
        pG = pb("pG", [128, 2, UG, 256])
        pM = pb("pM", [128, 2, 512])

        consts = sem("consts")
        raw_in = [sem(f"raw_in{r}") for r in range(RAW)]
        tab_high = sem("tab_high")
        tab_done = sem("tab_done")
        weights_in = sem("weights_in")
        wx_added = sem("wx_added")
        idx_in = [sem("idx_in0"), sem("idx_in1")]
        want_in = sem("want_in")
        gathered = [[sem(f"gathered{t}_{c}") for c in range(TQ)] for t in range(2)]
        dense_in = [sem("dense_in0"), sem("dense_in1")]
        columns_act = sem("columns_act")
        columns_dve = sem("columns_dve")
        distances = sem("distances")
        feat_done = sem("feat_done")
        feat_high = sem("feat_high")
        feat_low = sem("feat_low")
        gram_done = sem("gram_done")
        gram_act = sem("gram_act")
        gram_dve = sem("gram_dve")
        halves_added = sem("halves_added")
        inter_done = sem("inter_done")
        packed_done = sem("packed_done")
        small_done = sem("small_done")
        small_read = sem("small_read")
        stored = sem("stored")
        NW = 7

        GATHERS = [min(4 * c + 4, NG) - max(4 * c, 1) for c in range(TQ)]

        CUT = tuple(USE[turns[t][-1]] + 1 for t in range(2))
        assert CUT[0] > USE[hots[-1]] and CUT[1] == FU
        LOW = [sum(x[0] == "turn" for x in USES[:v + 1]) for v in range(FU)]

        def wait_unit_read(eng, p, n):
            eng.wait_ge(gram_act, p * (2 * TU) + n + 1)
            eng.wait_ge(gram_dve, p * (2 * TU) + n + 1)

        def read_unit(eng, copy, p, t, u, quads, first, done):
            n = t * TU + u
            if u == 0 and (t or not first):
                eng.wait_ge(inter_done, p * 2 + t)
            eng.wait_ge(gram_done, p * (2 * TU) + n + 1)
            for a in quads:
                rows = slice(a * PAD, a * PAD + PAD)
                part = pG[rows, n % 2, :, 0:2 * QUADS * FW].rearrange("p g (l q j) -> p l g q j", l=2, q=QUADS)
                dst = gram[rows, :, :, UG * u:UG * u + UG].rearrange("p l j g -> p l g j")
                last = copy(dst, part[:, :, :, a, 0:FEATS])
            last.then_inc(done, 1)

        def wait_built(eng, p, n):
            mine = BUILT[BUILDER[n]]
            eng.wait_ge(columns_act if BUILDER[n] == "act" else columns_dve, p * len(mine) + mine.index(n) + 1)

        def wait_columns_free(eng, p, n, very_first):
            eng.wait_ge(want_in, p * 16 + 16)
            if n >= RING:
                eng.wait_ge(feat_done, p * FU + USE["hot", n - RING] + 1)
            elif not very_first:
                v = max(m for m in range(NHOT) if (m - n) % RING == 0)
                eng.wait_ge(feat_done, (p - 1) * FU + USE["hot", v] + 1)

        block = ctx.enter_context(nc.Block())

        @block.sync
        def _(sp):
            def load_idx(p, t):
                sp.dma_start(idx[:, t, :], ids[bass.ds(p * PB + t * TB, TB), :]).then_inc(idx_in[t], 16)

            def load_dense(p, t):
                sp.dma_start(emb[:, t, 0, :], x[bass.ds(p * PB + t * TB, TB), :]).then_inc(dense_in[t], 16)

            for t in range(2):
                load_idx(0, t)
            for n in range(NHOT):
                if n >= RAW:
                    sp.wait_ge(tab_done, 2 + n - RAW + 1)
                sp.dma_start(raw[n % RAW].rearrange("p (c d) -> p c d", d=D),
                             hot_tables[n].rearrange("(p c) d -> p c d", c=ROW_CHUNKS)).then_inc(raw_in[n % RAW], 16)
                if n == 1:
                    for t in range(2):
                        load_dense(0, t)
            sp.wait_ge(tab_done, 2 + NHOT)
            sp.dma_start(wz_sb[:], wz.rearrange("(c p) n -> p c n", p=128)).then_inc(weights_in, 16)
            sp.dma_start(wx_sb[:], w1[0:D, :]).then_inc(weights_in, 16)
            sp.dma_start(wx2, w1[D + NPAIR:D + NPAIR + D, :]).then_inc(weights_in, 16)
            sp.dma_start(w2_sb[:], w2.rearrange("(c p) n -> p c n", p=128)).then_inc(weights_in, 16)
            sp.dma_start(w3_sb[:], w3[:, :]).then_inc(weights_in, 16)
            sp.dma_start(b1_sb[:], b1[:, :]).then_inc(weights_in, 16)
            sp.dma_start(b2_sb[:], b2[:, :]).then_inc(weights_in, 16)
            with sp.Fori(1, PAIRS) as p:
                sp.wait_ge(feat_done, p * FU + (CUT[0] - FU))
                load_idx(p, 0)
                load_dense(p, 0)
                sp.wait_ge(feat_done, p * FU)
                load_idx(p, 1)
                load_dense(p, 1)

        @block.gpsimd
        def _(pool):
            def gather(t):
                for f in range(NG - 1):
                    pool.indirect_dma_start(
                        out=emb[:, t, 1 + f, :], out_offset=None, in_=tables[f][:, :],
                        in_offset=bass.IndirectOffsetOnAxis(ap=idx[:, t, f:f + 1], axis=0),
                    ).then_inc(gathered[t][(1 + f) // 4], 16)

            pool.iota(row0[:], [[0, 1]], channel_multiplier=ROW_CHUNKS,
                      allow_small_or_imprecise_dtypes=True).then_inc(consts, 1)
            pool.iota(minus_row[:], [[-1, ROW_CHUNKS]], channel_multiplier=-ROW_CHUNKS,
                      allow_small_or_imprecise_dtypes=True).then_inc(consts, 1)
            pool.memset(ident[:], 0.0).then_inc(consts, 1)
            pool.wait_ge(consts, 3)
            pool.affine_select(out=ident[:], in_=ident[:], compare_op=ALU.not_equal, fill=1.0, base=0,
                               pattern=[[-1, 128]], channel_multiplier=1).then_inc(consts, 1)
            emb_free = pool.alloc_register("emb_free")
            pool.reg_mov(emb_free, CUT[0])
            for t in range(2):
                pool.wait_ge(idx_in[t], 16)
                gather(t)
            with pool.Fori(1, PAIRS) as p:
                for t in range(2):
                    pool.wait_ge(idx_in[t], p * 16 + 16)
                    pool.wait_ge(feat_done, emb_free)
                    pool.reg_add(emb_free, emb_free, FU - CUT[0] if t == 0 else CUT[0])
                    gather(t)

        @block.tensor
        def _(pe):
            def wait_feature_bank(p, u, first):
                v = u - 2 if u >= 2 else (FU - 1 if (FU - 1 - u) % 2 == 0 else FU - 2)
                q = p if u >= 2 else p - 1
                if u < 2 and first:
                    return
                if USES[v][0] == "hot":
                    pe.wait_ge(feat_high, q * FU + v + 1)
                else:
                    pe.wait_ge(feat_low, q * (2 * TQ) + LOW[v])

            def look_up(p, n, first):
                u = USE["hot", n]
                if first:
                    pe.wait_ge(tab_done, 2 + n + 1)
                wait_built(pe, p, n)
                wait_feature_bank(p, u, first)
                for part in range(2):
                    for c in range(ROW_CHUNKS):
                        last = pe.matmul(pF[:, u % 2, part * PB:(part + 1) * PB], tab[:, n, part, c, :],
                                         onehot[:, n % RING, c, :], start=(c == 0), stop=(c == ROW_CHUNKS - 1))
                last.then_inc(feat_done, 1)

            def turn(p, t, c, first):
                u = USE["turn", t, c]
                pe.wait_ge(gathered[t][c], p * (16 * GATHERS[c]) + 16 * GATHERS[c])
                if c == 0:
                    pe.wait_ge(dense_in[t], p * 16 + 16)
                wait_feature_bank(p, u, first)
                for f in range(4 * c, min(4 * c + 4, NG)):
                    last = pe.transpose(pF[:, u % 2, (f % 4) * 128:(f % 4) * 128 + 128], emb[:, t, f, :], ident[:])
                last.then_inc(feat_done, 1)

            def gram_unit(p, t, u, first):
                n = t * TU + u
                if u == 0:
                    pe.wait_ge(feat_high, p * FU + CUT[t])
                    pe.wait_ge(feat_low, p * (2 * TQ) + TQ * (t + 1))
                if n >= 2 or not first:
                    wait_unit_read(pe, p if n >= 2 else p - 1, (n - 2) % (2 * TU))
                for g in range(UG):
                    left = embT[:, 0, t, UG * u + g, :, :].rearrange("p q f -> p (q f)")
                    right = embT[:, :, t, UG * u + g, :, 0:FW]
                    last = pe.matmul(pG[:, n % 2, g, 0:2 * QUADS * FW], left, right,
                                     start=(g % 2 == 0), stop=True, skip_group_check=True)
                last.then_inc(gram_done, 1)

            def small(m, k, very_first, part=None):
                def products(pairs):
                    half = len(pairs) // 2
                    at = {None: range(len(pairs)), 0: range(half), 1: range(half, len(pairs))}[part]
                    return [pe.matmul(bank, pairs[i][0], pairs[i][1], start=(i == 0), stop=(i == len(pairs) - 1))
                            for i in at][-1]

                v = k - 2 if k >= 2 else (SU - 1 if (SU - 1 - k) % 2 == 0 else SU - 2)
                if part != 1 and (k >= 2 or not very_first):
                    pe.wait_ge(small_read, (m if k >= 2 else m - 1) * SU + v + 1)
                bank = pM[:, k % 2, 0:PB]
                if k < 2:
                    pe.wait_ge(packed_done, m * 2 + k + 1)
                    for c in range(PAIR_CHUNKS):
                        last = pe.transpose(pM[:, k % 2, c * 128:c * 128 + 128],
                                            packed[:, c * 128:c * 128 + 128], ident[:])
                elif k < 2 + N1:
                    n = k - 2
                    cols = slice(n * 128, n * 128 + 128)
                    if part != 1:
                        pe.wait_ge(small_read, m * SU + 2)
                    last = products([(wx_sb[:, cols], xT[:, bass.ds((m % 2) * PB, PB)])]
                                    + [(wz_sb[:, c, cols], packT[:, c, :]) for c in range(PAIR_CHUNKS)])
                elif k < 2 + N1 + N2:
                    if part != 1:
                        pe.wait_ge(small_read, m * SU + 2 + N1)
                    n = k - 2 - N1
                    last = products([(w2_sb[:, c, n * 128:n * 128 + 128], h1[:, c, :]) for c in range(N1)])
                else:
                    pe.wait_ge(small_read, m * SU + SU - 1)
                    for c in range(N2):
                        last = pe.matmul(bank[0:1, :], w3_sb[:, c:c + 1], h2[:, c, :],
                                         start=(c == 0), stop=(c == N2 - 1))
                if part != 0:
                    last.then_inc(small_done, 1)

            def pair(p, first, second=False, order=SCHEDULE):
                for what, *at in order:
                    if what == "hot":
                        look_up(p, *at, first)
                    elif what == "turn":
                        turn(p, *at, first)
                    elif what == "gram":
                        gram_unit(p, *at, first)
                    elif what == "layers":
                        layers(*at)
                    elif what == "begin" and not first:
                        small(p - 1, *at, second, 0)
                    elif not first:
                        small(p - 1, *at, second, 1 if ("begin", *at) in order else None)

            def layers(t, k):
                base = (PAIRS - 1) * SU + t * SL
                pe.wait_ge(small_read, base + max(k - 1, 0))
                bank = pM[:, k % 2, 0:TB]
                cols = slice(t * TB, (t + 1) * TB)
                if k == 0:
                    pe.wait_ge(packed_done, (PAIRS - 1) * 2 + t + 1)
                    for c in range(PAIR_CHUNKS):
                        last = pe.transpose(pM[:, k % 2, c * 128:c * 128 + 128],
                                            packed[:, c * 128:c * 128 + 128], ident[:])
                elif k < 1 + N1:
                    n = k - 1
                    w = slice(n * 128, n * 128 + 128)
                    pe.wait_ge(small_read, base + 1)
                    at = ((PAIRS - 1) % 2) * PB + t * TB
                    pe.matmul(bank, wx_sb[:, w], xT[:, at:at + TB], start=True, stop=False)
                    for c in range(PAIR_CHUNKS):
                        last = pe.matmul(bank, wz_sb[:, c, w], packT[:, c, cols], start=False,
                                         stop=(c == PAIR_CHUNKS - 1))
                elif k < 1 + N1 + N2:
                    pe.wait_ge(small_read, base + 1 + N1)
                    n = k - 1 - N1
                    for c in range(N1):
                        last = pe.matmul(bank, w2_sb[:, c, n * 128:n * 128 + 128], h1[:, c, cols],
                                         start=(c == 0), stop=(c == N1 - 1))
                else:
                    pe.wait_ge(small_read, base + SL - 1)
                    for c in range(N2):
                        last = pe.matmul(bank[0:1, :], w3_sb[:, c:c + 1], h2[:, c, cols],
                                         start=(c == 0), stop=(c == N2 - 1))
                last.then_inc(small_done, 1)

            pe.wait_ge(consts, 4)
            pair(0, True)
            pe.wait_ge(weights_in, 16 * NW)
            pe.wait_ge(wx_added, 1)
            pair(1, False, True)
            with pe.Fori(2, PAIRS - 1) as p:
                pair(p, False)
            pair(PAIRS - 1, False, order=PE_LAST)

        @block.scalar
        def _(act):
            def copy(dst, src):
                return act.activation(dst, src, ACT.Copy)

            def load_want(p):
                src = hot_ids[:, bass.ds(p * PB, PB)]
                src = bass.AP(src.tensor, src.offset, [[0, HROWS]] + list(src.ap))
                act.dma_start(want[:], src).then_inc(want_in, 16)

            def read_hot(p, n):
                u = USE["hot", n]
                act.wait_ge(feat_done, p * FU + u + 1)
                for part in range(2):
                    last = copy(embT[:, part, :, :, :, NG + n].rearrange("p t g q -> p t q g"),
                                pF[:, u % 2, part * PB:(part + 1) * PB].rearrange("p (t q g) -> p t q g", t=2, q=QUADS))
                last.then_inc(feat_high, 1)

            def read_high(p, t, c):
                u = USE["turn", t, c]
                act.wait_ge(feat_done, p * FU + u + 1)
                n = min(4, NG - 4 * c)
                src = pF[:, u % 2, 0:n * 128].rearrange("p (f b) -> p f b", b=TB)
                if c == 0:
                    copy(xT[:, bass.ds((p % 2) * PB + t * TB, TB)], src[:, 0, :])
                copy(embT[:, 0, t, :, :, 4 * c:4 * c + n].rearrange("p g q f -> p f q g"),
                     src.rearrange("p f (q g) -> p f q g", q=QUADS)).then_inc(feat_high, 1)

            def read_small(m, k, very_first):
                act.wait_ge(small_done, m * SU + k + 1)
                bank = pM[:, k % 2, 0:PB]
                if k < 2:
                    copy(packT[:, :, k * TB:(k + 1) * TB],
                         pM[:, k % 2, 0:PAIR_CHUNKS * 128].rearrange("p (c b) -> p c b", b=TB)).then_inc(small_read, 1)
                elif k < 2 + N1:
                    n = k - 2
                    act.activation(h1[:, n, :], bank, ACT.Relu, bias=b1_sb[:, n:n + 1]).then_inc(small_read, 1)
                elif k < 2 + N1 + N2:
                    n = k - 2 - N1
                    act.activation(h2[:, n, :], bank, ACT.Relu, bias=b2_sb[:, n:n + 1]).then_inc(small_read, 1)
                else:
                    if not very_first:
                        act.wait_ge(stored, m * 16)
                    copy(y[:], bank[0:1, :]).then_inc(small_read, 1)
                    act.wait_ge(small_read, m * SU + SU)
                    act.dma_start(out[bass.ds(m * PB, PB), :].rearrange("b n -> n b"), y[:]).then_inc(stored, 16)

            def read_layers(t, k):
                base = (PAIRS - 1) * SU + t * SL
                act.wait_ge(small_done, base + k + 1)
                bank = pM[:, k % 2, 0:TB]
                cols = slice(t * TB, (t + 1) * TB)
                if k == 0:
                    copy(packT[:, :, cols],
                         pM[:, k % 2, 0:PAIR_CHUNKS * 128].rearrange("p (c b) -> p c b", b=TB)).then_inc(small_read, 1)
                elif k < 1 + N1:
                    n = k - 1
                    act.activation(h1[:, n, cols], bank, ACT.Relu, bias=b1_sb[:, n:n + 1]).then_inc(small_read, 1)
                elif k < 1 + N1 + N2:
                    n = k - 1 - N1
                    act.activation(h2[:, n, cols], bank, ACT.Relu, bias=b2_sb[:, n:n + 1]).then_inc(small_read, 1)
                else:
                    if t == 0:
                        act.wait_ge(stored, (PAIRS - 1) * 16)
                    copy(y[:, cols], bank[0:1, :]).then_inc(small_read, 1)
                    act.wait_ge(small_read, base + SL)
                    at = (PAIRS - 1) * PB + t * TB
                    act.dma_start(out[at:at + TB, :].rearrange("b n -> n b"), y[:, cols]).then_inc(stored, 16)

            def build(p, n, half, very_first):
                at = [half * ROW_CHUNKS // 2, (half + 1) * ROW_CHUNKS // 2]
                if half == 0:
                    wait_columns_free(act, p, n, very_first)
                for c in range(*at):
                    last = act.activation(onehot[:, n % RING, c, :], want[:, n, :], ACT.Abs,
                                          bias=minus_row[:, c:c + 1])
                last.then_inc(distances, 1)
                act.wait_ge(distances, p * (2 * len(BUILT["act"])) + (2 * BUILT["act"].index(n) + half + 1))
                both = onehot[:, n % RING, at[0]:at[1], :]
                last = act.activation(both, both.bitcast(f32), ACT.Relu, scale=-1.0, bias=1.0)
                if half:
                    last.then_inc(columns_act, 1)

            def pair(p, first, second=False, last=False, order=ACT_ORDER):
                if not first:
                    act.wait_ge(gram_done, p * (2 * TU))
                for what, *at in order:
                    if what == "hot":
                        read_hot(p, *at)
                    elif what == "want":
                        if not last:
                            for built in BUILT.values():
                                if built:
                                    wait_built(act, p, built[-1])
                            load_want(p + 1)
                    elif what == "build":
                        build(p, *at, False)
                    elif what == "ahead":
                        if not last:
                            build(p + 1, *at, False)
                    elif what == "turn":
                        read_high(p, *at)
                    elif what == "gram":
                        read_unit(act, copy, p, *at, range(QUADS - DVE_QUADS[at[1]]), first, gram_act)
                    elif what == "layers":
                        read_layers(*at)
                    elif not first:
                        read_small(p - 1, *at, second)

            load_want(0)
            for n in range(NHOT):
                act.wait_ge(raw_in[n % RAW], 16 * (n // RAW + 1))
                copy(tab[:, n, 0, :, :].rearrange("p c d -> p (c d)"), raw[n % RAW]).then_inc(tab_high, 1)
            act.wait_ge(consts, 4)
            pair(0, True, order=ACT_FIRST)
            act.wait_ge(weights_in, 16 * NW)
            act.wait_ge(wx_added, 1)
            pair(1, False, True)
            with act.Fori(2, PAIRS - 1) as p:
                pair(p, False)
            pair(PAIRS - 1, False, False, True, order=ACT_LAST)
            act.wait_ge(stored, 16 * (PAIRS + 1))

        @block.vector
        def _(dve):
            def build(p, n, half, very_first):
                if half == 0:
                    wait_columns_free(dve, p, n, very_first)
                for c in range(half * ROW_CHUNKS // 2, (half + 1) * ROW_CHUNKS // 2):
                    last = dve.tensor_scalar(onehot[:, n % RING, c, :], want[:, n, :], float(c), row0[:, 0:1],
                                             ALU.subtract, ALU.is_equal)
                if half:
                    last.then_inc(columns_dve, 1)

            def read_low(p, t, c):
                u = USE["turn", t, c]
                dve.wait_ge(feat_high, p * FU + u + 1)
                n = min(4, NG - 4 * c)
                src = pF[:, u % 2, 0:n * 128].rearrange("p (f q g) -> p f q g", f=n, q=QUADS)
                high, low = (embT[:, part, t, :, :, 4 * c:4 * c + n].rearrange("p g q f -> p f q g")
                             for part in range(2))
                dve.tensor_tensor(low, src, high.bitcast(f32), ALU.subtract).then_inc(feat_low, 1)

            def pack(p, t, first):
                wait_unit_read(dve, p, t * TU + TU - 1)
                dve.scalar_tensor_tensor(out=gram[:, 1, :, :], in0=gram[:, 0, :, :], scalar=0.5, in1=gram[:, 1, :, :],
                                         op0=ALU.mult, op1=ALU.add).then_inc(halves_added, 1)
                dve.wait_ge(halves_added, p * 2 + t + 1)
                if t or not first:
                    dve.wait_ge(packed_done, p * 2 + t)
                dve.transpose(inter[:, 0:FEATS * PAD], gram[:, 1, :, :]).then_inc(inter_done, 1)
                dve.wait_ge(inter_done, p * 2 + t + 1)
                if t:
                    dve.wait_ge(small_done, p * SU + 1)
                elif not first:
                    dve.wait_ge(small_done, (p - 1) * SU + 2)
                for slot, j0, i0, dims in COPIES:
                    n = [d[2] for d in dims]
                    src = inter[:, :]
                    ji = bass.AP(src.tensor, src.offset + j0 * PAD + i0,
                                 [src.ap[0]] + [[dj * PAD + di, m] for dj, di, m in dims])
                    ij = bass.AP(src.tensor, src.offset + i0 * PAD + j0,
                                 [src.ap[0]] + [[di * PAD + dj, m] for dj, di, m in dims])
                    dst = packed[:, slot:slot + int(np.prod(n))]
                    names = "abc"[:len(n)]
                    dst = dst.rearrange(f"p ({' '.join(names)}) -> p {' '.join(names)}", **dict(zip(names, n)))
                    last = dve.tensor_add(dst, ji, ij)
                last.then_inc(packed_done, 1)

            def pair(p, first, last):
                for what, *at in DVE_ORDER:
                    if what == "build":
                        build(p, *at, False)
                    elif what == "ahead":
                        if not last:
                            build(p + 1, *at, False)
                    elif what == "turn":
                        read_low(p, *at)
                    elif what == "gram":
                        read_unit(dve, dve.tensor_copy, p, *at, range(QUADS - DVE_QUADS[at[1]], QUADS), first, gram_dve)
                    elif what == "pack" and at[0] == 0:
                        pack(p, 0, first)
                    elif what == "pack" and not first:
                        pack(p - 1, 1, False)

            dve.memset(embT[:, :, :, :, :, FEATS:PAD].rearrange("p l t g q f -> p (l t g q) f").bitcast(f32), 0.0).then_inc(tab_done, 1)
            dve.memset(packed[:, len(SLOTS):], 0.0)
            dve.memset(inter[:, FEATS * PAD:], 0.0).then_inc(tab_done, 1)
            for n in range(NHOT):
                dve.wait_ge(tab_high, n + 1)
                dve.tensor_tensor(tab[:, n, 1, :, :].rearrange("p c d -> p (c d)"), raw[n % RAW],
                                  tab[:, n, 0, :, :].rearrange("p c d -> p (c d)").bitcast(f32),
                                  ALU.subtract).then_inc(tab_done, 1)
                if n == 0:
                    dve.wait_ge(consts, 4)
                if n < RING:
                    build(0, n, 0, True)
                    build(0, n, 1, True)
            pair(0, True, False)
            dve.wait_ge(weights_in, 16 * NW)
            dve.tensor_add(wx_sb[:], wx_sb[:], wx2).then_inc(wx_added, 1)
            with dve.Fori(1, PAIRS - 1) as p:
                pair(p, False, False)
            pair(PAIRS - 1, False, True)
            pack(PAIRS - 1, 1, False)


def kernel(**inputs):
    import concourse.bacc as bacc
    from concourse.bass_utils import run_bass_kernel_spmd

    a = {k: np.asarray(v) for k, v in inputs.items()}
    w1 = a["W_top1"]
    D = a["r_dense_features"].shape[1]
    hot, cold = split_fields([a[f"tbl_{f}"].shape[0] for f in range(FIELDS)])
    order = [0] + [1 + f for f in cold + hot]
    wz = np.zeros((PAIR_CHUNKS * 128, w1.shape[1]), w1.dtype)
    for slot, pair in enumerate(SLOTS):
        if pair is not None:
            j, i = sorted(order[f] for f in pair)
            wz[slot] = w1[D + j * FEATS - j * (j + 1) // 2 + i - j - 1]

    def by_partition(v):
        return v.reshape(-1, 128).T

    arrays = {"x": a["r_dense_features"], "ids": a["ids"][:, cold], "hot_ids": a["ids"][:, hot].T}
    for f in cold + hot:
        arrays[f"tbl_{f}"] = a[f"tbl_{f}"]
    arrays.update(wz=wz, w1=w1, b1=by_partition(a["b_top1"]), w2=a["W_top2"], b2=by_partition(a["b_top2"]),
                  w3=by_partition(a["W_top3"]))
    arrays = {k: np.ascontiguousarray(v) for k, v in arrays.items()}
    nc = bacc.Bacc("TRN2", target_bir_lowering=False, num_devices=1)
    aps = {k: nc.dram_tensor(f"in_{k}", v.shape, mybir.dt.from_np(v.dtype), kind="ExternalInput").ap()
           for k, v in arrays.items()}
    out = nc.dram_tensor("out_y", (a["ids"].shape[0], 1), mybir.dt.float32, kind="ExternalOutput").ap()
    dlrm_tower(nc, aps["x"], aps["ids"], aps["hot_ids"], [aps[f"tbl_{f}"] for f in cold],
               [aps[f"tbl_{f}"] for f in hot], aps["wz"], aps["w1"], aps["b1"], aps["w2"], aps["b2"],
               aps["w3"], out)
    r = run_bass_kernel_spmd(nc, [{f"in_{k}": v for k, v in arrays.items()}], core_ids=[0])
    return r.results[0]["out_y"]
```
